# Optimizing a Trainium2 kernel written in Bass

```python
import numpy as np
import jax
import jax.numpy as jnp

def _softmax(x, axis=-1):
    return jax.nn.softmax(x, axis=axis)

def _gelu(x):
    return jax.nn.gelu(x, approximate=True)

def _silu(x):
    return jax.nn.silu(x)

def _sigmoid(x):
    return jax.nn.sigmoid(x)

def _layernorm(x, axis=-1, eps=1e-05):
    m = jnp.mean(x, axis=axis, keepdims=True)
    v = jnp.var(x, axis=axis, keepdims=True)
    return (x - m) / jnp.sqrt(v + eps)

def _scatter_add(tgt, idx, src, axis=0):
    return tgt.at[idx].add(src)

def _segment_sum(src, seg, n):
    return jax.ops.segment_sum(src, seg, n)
kernel_name = 'mk_gnn_ffn_d1_gnn_r64_fa9f5a'

def setup_inputs(seed: int=0):
    np.random.seed(seed)
    _w = jnp.asarray

    def _rec_inputs():
        import jax
        import jax.numpy as jnp
        _gk = jax.random.key(seed)
        x = -0.0001126 + 1 * jax.random.normal(jax.random.fold_in(_gk, 1), (10000, 768), jnp.float32)
        src = jax.random.randint(jax.random.fold_in(_gk, 2), (5000,), 0, 10000, jnp.int32)
        dst = jnp.minimum((10000 * jax.random.uniform(jax.random.fold_in(_gk, 3), (5000,)) ** 2.0).astype(jnp.int32), 9999)
        _o = jnp.argsort(dst, stable=True)
        src = src[_o]
        dst = dst[_o]
        return (x, src, dst)
    x, src, dst = _rec_inputs()

    def _L0_gnn_setup():
        import jax, jax.numpy as jnp
        import numpy as np
        N, E, DM, H, L = (10000, 2500, 768, 8, 2)
        HD = DM // H
        LN_EPS = 1e-05
        SLOPE = 0.2

        def layer_norm(x, w, b):
            mu = jnp.mean(x, axis=-1, keepdims=True)
            var = jnp.mean(jnp.square(x - mu), axis=-1, keepdims=True)
            return (x - mu) * jax.lax.rsqrt(var + LN_EPS) * w + b

        def gatv2_layer(x, Ws, bs, Wd, bd, attn, src, dst):
            hs = (x @ Ws + bs).reshape(N, H, HD)
            hd = (x @ Wd + bd).reshape(N, H, HD)
            hs_e = hs[src]
            e = jax.nn.leaky_relu(hs_e + hd[dst], SLOPE)
            logits = jnp.einsum('ehd,hd->eh', e, attn)
            m = jax.ops.segment_max(logits, dst, num_segments=N)
            ex = jnp.exp(logits - m[dst])
            s = jax.ops.segment_sum(ex, dst, num_segments=N)
            alpha = ex / s[dst]
            out = jax.ops.segment_sum(alpha[..., None] * hs_e, dst, num_segments=N)
            return jax.nn.elu(out).reshape(N, DM)
        key = jax.random.key(seed)
        ks = jax.random.split(key, 12)
        xav = 1.0 / np.sqrt(DM)
        return {'x': jax.random.normal(ks[0], (N, DM), jnp.float32), 'Wsrc': jax.random.uniform(ks[1], (L, DM, DM), jnp.float32, -xav, xav), 'bsrc': jnp.zeros((L, DM), jnp.float32), 'Wdst': jax.random.uniform(ks[2], (L, DM, DM), jnp.float32, -xav, xav), 'bdst': jnp.zeros((L, DM), jnp.float32), 'attn': jax.random.normal(ks[3], (L, H, HD), jnp.float32) * (1.0 / np.sqrt(HD)), 'ln_w': jnp.ones((L, DM), jnp.float32), 'ln_b': jnp.zeros((L, DM), jnp.float32), 'on_w': jnp.ones((DM,), jnp.float32), 'on_b': jnp.zeros((DM,), jnp.float32), 'src': jax.random.randint(ks[4], (E,), 0, N, jnp.int32), 'dst': jax.random.randint(ks[5], (E,), 0, N, jnp.int32)}
    _L0_gnn_all = _L0_gnn_setup()
    _L0_gnn_in = {k: v for k, v in _L0_gnn_all.items() if k in ('Wsrc', 'bsrc', 'Wdst', 'bdst', 'attn', 'ln_w', 'ln_b', 'on_w', 'on_b')}
    del _L0_gnn_all

    def _L0_ffn_setup():
        import jax, jax.numpy as jnp
        import numpy as np
        QN, QP = (-8, 7)

        def round_pass(x):
            return x + jax.lax.stop_gradient(jnp.round(x) - x)

        def _quant_act(x, alpha_a):
            a = alpha_a.mean()
            return round_pass(jnp.clip(x / a, QN, QP))

        def _quant_w(w, alpha_w):
            return round_pass(jnp.clip(w / alpha_w[:, None], QN, QP))
        key = jax.random.key(seed)
        ks = jax.random.split(key, 9)
        B, S, D, H = (16, 1024, 768, 48)

        def unif(k, shape):
            return jax.random.uniform(k, shape, jnp.float32, 0.02, 0.1)
        return {'x0': jax.random.normal(ks[0], (B, S, D), jnp.float32), 'w1': jax.random.normal(ks[1], (H, D), jnp.float32) * 0.02, 'b1': jax.random.normal(ks[2], (H,), jnp.float32) * 0.02, 'alpha_w1': unif(ks[3], (H,)), 'alpha_a1': unif(ks[4], (D,)), 'w2': jax.random.normal(ks[5], (D, H), jnp.float32) * 0.02, 'b2': jax.random.normal(ks[6], (D,), jnp.float32) * 0.02, 'alpha_w2': unif(ks[7], (D,)), 'alpha_a2': unif(ks[8], (H,))}
    _L0_ffn_all = _L0_ffn_setup()
    _L0_ffn_in = {k: v for k, v in _L0_ffn_all.items() if k in ('w1', 'b1', 'alpha_w1', 'alpha_a1', 'w2', 'b2', 'alpha_w2', 'alpha_a2')}
    del _L0_ffn_all
    return {'x': x, 'src': src, 'dst': dst, 'L0_gnn_Wsrc': _L0_gnn_in['Wsrc'], 'L0_gnn_bsrc': _L0_gnn_in['bsrc'], 'L0_gnn_Wdst': _L0_gnn_in['Wdst'], 'L0_gnn_bdst': _L0_gnn_in['bdst'], 'L0_gnn_attn': _L0_gnn_in['attn'], 'L0_gnn_ln_w': _L0_gnn_in['ln_w'], 'L0_gnn_ln_b': _L0_gnn_in['ln_b'], 'L0_gnn_on_w': _L0_gnn_in['on_w'], 'L0_gnn_on_b': _L0_gnn_in['on_b'], 'L0_ffn_w1': _L0_ffn_in['w1'], 'L0_ffn_b1': _L0_ffn_in['b1'], 'L0_ffn_alpha_w1': _L0_ffn_in['alpha_w1'], 'L0_ffn_alpha_a1': _L0_ffn_in['alpha_a1'], 'L0_ffn_w2': _L0_ffn_in['w2'], 'L0_ffn_b2': _L0_ffn_in['b2'], 'L0_ffn_alpha_w2': _L0_ffn_in['alpha_w2'], 'L0_ffn_alpha_a2': _L0_ffn_in['alpha_a2']}

def reference(x, src, dst, L0_gnn_Wsrc, L0_gnn_bsrc, L0_gnn_Wdst, L0_gnn_bdst, L0_gnn_attn, L0_gnn_ln_w, L0_gnn_ln_b, L0_gnn_on_w, L0_gnn_on_b, L0_ffn_w1, L0_ffn_b1, L0_ffn_alpha_w1, L0_ffn_alpha_a1, L0_ffn_w2, L0_ffn_b2, L0_ffn_alpha_w2, L0_ffn_alpha_a2):
    import jax
    import jax.numpy as jnp

    def _L0_gnn_ref(x, Wsrc, bsrc, Wdst, bdst, attn, ln_w, ln_b, on_w, on_b, src, dst):
        import jax, jax.numpy as jnp
        import numpy as np
        N, E, DM, H, L = (10000, 2500, 768, 8, 2)
        HD = DM // H
        LN_EPS = 1e-05
        SLOPE = 0.2

        def layer_norm(x, w, b):
            mu = jnp.mean(x, axis=-1, keepdims=True)
            var = jnp.mean(jnp.square(x - mu), axis=-1, keepdims=True)
            return (x - mu) * jax.lax.rsqrt(var + LN_EPS) * w + b

        def gatv2_layer(x, Ws, bs, Wd, bd, attn, src, dst):
            hs = (x @ Ws + bs).reshape(N, H, HD)
            hd = (x @ Wd + bd).reshape(N, H, HD)
            hs_e = hs[src]
            e = jax.nn.leaky_relu(hs_e + hd[dst], SLOPE)
            logits = jnp.einsum('ehd,hd->eh', e, attn)
            m = jax.ops.segment_max(logits, dst, num_segments=N)
            ex = jnp.exp(logits - m[dst])
            s = jax.ops.segment_sum(ex, dst, num_segments=N)
            alpha = ex / s[dst]
            out = jax.ops.segment_sum(alpha[..., None] * hs_e, dst, num_segments=N)
            return jax.nn.elu(out).reshape(N, DM)
        h = x
        for l in range(L):
            h_new = gatv2_layer(h, Wsrc[l], bsrc[l], Wdst[l], bdst[l], attn[l], src, dst)
            h = layer_norm(h_new + h, ln_w[l], ln_b[l])
        return layer_norm(h, on_w, on_b)

    def _L0_ffn_ref(x0, w1, b1, alpha_w1, alpha_a1, w2, b2, alpha_w2, alpha_a2):
        import jax, jax.numpy as jnp
        import numpy as np
        QN, QP = (-8, 7)

        def round_pass(x):
            return x + jax.lax.stop_gradient(jnp.round(x) - x)

        def _quant_act(x, alpha_a):
            a = alpha_a.mean()
            return round_pass(jnp.clip(x / a, QN, QP))

        def _quant_w(w, alpha_w):
            return round_pass(jnp.clip(w / alpha_w[:, None], QN, QP))
        xq = _quant_act(x0, alpha_a1)
        wq1 = _quant_w(w1, alpha_w1)
        x1 = jnp.einsum('bsd,hd->bsh', xq, wq1)
        x1 = x1 * alpha_w1 * alpha_a1.mean() + b1
        x1 = jax.nn.gelu(x1, approximate=False)
        x1 = jnp.clip(x1, -10.0, 10.0)
        hq = _quant_act(x1, alpha_a2)
        wq2 = _quant_w(w2, alpha_w2)
        x2 = jnp.einsum('bsh,dh->bsd', hq, wq2)
        x2 = x2 * alpha_w2 * alpha_a2.mean() + b2
        return x2
    x = x + _L0_gnn_ref(_layernorm(x, axis=-1), L0_gnn_Wsrc, L0_gnn_bsrc, L0_gnn_Wdst, L0_gnn_bdst, L0_gnn_attn, L0_gnn_ln_w, L0_gnn_ln_b, L0_gnn_on_w, L0_gnn_on_b, src, dst)
    x = x + _L0_ffn_ref(_layernorm(x, axis=-1)[None], L0_ffn_w1, L0_ffn_b1, L0_ffn_alpha_w1, L0_ffn_alpha_a1, L0_ffn_w2, L0_ffn_b2, L0_ffn_alpha_w2, L0_ffn_alpha_a2)[0]
    return x

_drawn_inputs = setup_inputs


def setup_inputs(seed=0):
    import zlib

    import numpy as np

    out = dict(_drawn_inputs(seed))
    spreads = {'L0_gnn_bsrc': (0.0, 0.1),
     'L0_gnn_bdst': (0.0, 2.0),
     'L0_gnn_ln_w': (1.0, 0.2),
     'L0_gnn_ln_b': (0.0, 0.1),
     'L0_gnn_on_w': (1.0, 0.2),
     'L0_gnn_on_b': (0.0, 0.1)}
    factors = {'L0_gnn_Wdst': 7.909,
     'L0_gnn_attn': 2.993,
     'L0_ffn_w1': 7.546,
     'L0_ffn_b1': 8.0,
     'L0_ffn_alpha_w1': 8.0,
     'L0_ffn_w2': 7.455,
     'L0_ffn_b2': 5.423,
     'L0_ffn_alpha_w2': 8.0,
     'L0_ffn_alpha_a2': 64.0,
     'L0_ffn_alpha_a1': 8.0}
    for name, (base, spread) in spreads.items():
        noise = np.random.default_rng([zlib.crc32(name.encode()), seed]).standard_normal(out[name].shape)
        drawn = base * np.exp(spread * noise) if base else spread * noise
        out[name] = jnp.asarray(drawn.astype(out[name].dtype))
    for name, factor in factors.items():
        out[name] = (out[name] * factor).astype(out[name].dtype)
    return out
```

```python
from contextlib import ExitStack

import concourse.bass as bass
from concourse import mybir

F32, F16, BF16, I32 = mybir.dt.float32, mybir.dt.float16, mybir.dt.bfloat16, mybir.dt.int32
ALU = mybir.AluOpType
ACT = mybir.ActivationFunctionType
AX_X = mybir.AxisListType.X

P = 128
EPS = 1e-5
SLOPE = 0.2
NO_NODE = 16384
OTHER_NODE = 32768
FAR = -1e30
H_SCALE = 16.0
W_SCALE = 64.0
Z_SCALE = 1.0 / (H_SCALE * W_SCALE)
ROUND = 12582912.0
QN, QP = -8.0, 7.0
UNROLL = 4


class Step:

    def __init__(self, k, r, unroll):
        self.k, self.r, self.unroll = k, r, unroll

    def of(self, ahead):
        return Step(self.k, self.r + ahead, self.unroll)

    @property
    def fixed(self):
        return isinstance(self.k, int)

    @property
    def n(self):
        return self.k * self.unroll + self.r

    def slot(self, slots):
        return self.r % slots

    def turn(self, slots):
        return self.k * (self.unroll // slots) + self.r // slots

    def inside(self, steps):
        return not self.fixed or 0 <= self.r < steps


def wait(eng, sem, count):
    if not isinstance(count, int) or count > 0:
        eng.wait_ge(sem, count)


def wait_apart(eng, passed, *waits):
    for sem, count in waits:
        wait(eng, sem, count)
    eng.sem_inc(passed, 1)


def pipeline(eng, body, first, steps, lead, tail, unroll=UNROLL):
    lo = (tail // unroll + 1) * unroll
    hi = (steps - lead) // unroll * unroll
    for i in range(first, lo):
        body(Step(0, i, unroll))
    with eng.Fori(lo // unroll, hi // unroll) as k:
        for u in range(unroll):
            body(Step(k, u, unroll))
    for i in range(hi, steps + tail):
        body(Step(0, i, unroll))


def rows(ap, row, count, width):
    return bass.AP(ap.tensor, ap.offset, [[row, count], [1, width]])


def replicated(ap, parts, width):
    return bass.AP(ap.tensor, ap.offset, [[0, parts], [1, width]])


def gat_and_quantised_ffn(nc, x, src, dst, Wsrc, bsrc, Wdst, bdst, attn, ln_w, ln_b, on_w, on_b,
                          w1, b1, alpha_w1, alpha_a1, w2, b2, alpha_w2, alpha_a2, out):
    N, D = x.shape
    E, = src.shape
    L = Wsrc.shape[0]
    H = attn.shape[1]
    HD = D // H
    F = w1.shape[0]
    KC = D // P
    HALF = D // 2
    EPT = P - 1
    ET = -(-E // EPT)
    NE = ET * EPT + P
    G = 2
    NB = -(-N // (P * G))
    LAST = N - (NB - 1) * P * G
    SORT_T = -(-E // P)
    assert D == KC * P and LAST % G == 0 and SORT_T * P + 1 <= NE and E % 8 == 0

    ctx = ExitStack()

    taken = []

    def sem(name):
        taken.append(nc.alloc_semaphore(name))
        return taken[-1]

    def end_phase():
        nc.clear_and_free_semaphores(taken)
        taken.clear()
        nc.all_engine_barrier()

    def sb(name, shape, dt=F32):
        return scope.enter_context(nc.sbuf_tensor(name, shape, dt))

    def ps(name, shape, dt=F32):
        return scope.enter_context(nc.psum_tensor(name, shape, dt))

    edge_src = nc.dram_tensor("edge_src", [NE, 1], I32, kind="Internal").ap()
    edge_dst = nc.dram_tensor("edge_dst", [NE, 1], I32, kind="Internal").ap()
    h_table = nc.dram_tensor("h_table", [N, D], F32, kind="Internal").ap()
    x_table = nc.dram_tensor("x_table", [N, D], F32, kind="Internal").ap()

    def flat(a):
        return a.rearrange("n o -> (n o)")

    with ctx:
        scope = ctx
        ident = sb("ident", [P, P])
        identb = sb("identb", [P, P], BF16)
        key_row = sb("key_row", [P, NE])
        border = sb("border", [H, NE])
        key_col = sb("key_col", [P, ET])
        src_idx = sb("src_idx", [P, ET], I32)
        dst_idx = sb("dst_idx", [P, ET], I32)
        out_idx = sb("out_idx", [P, ET], I32)

        with ExitStack() as scope:
            s_const, s_pad, s_in, s_fill, s_zero = (sem(n) for n in ("p_const", "p_pad", "p_in", "p_fill", "p_zero"))
            s_f, s_tr, s_col, s_cnt, s_flag = (sem(n) for n in ("p_f", "p_tr", "p_col", "p_cnt", "p_flag"))
            s_row, s_v, s_a, s_b, s_rank = (sem(n) for n in ("p_row", "p_v", "p_a", "p_b", "p_rank"))
            s_stage, s_put, s_sorted = (sem(n) for n in ("p_stage", "p_put", "p_sorted"))
            s_win, s_key, s_wf, s_wt, s_wc, s_g = (sem(n) for n in ("p_win", "p_key", "p_wf", "p_wt", "p_wc", "p_g"))
            s_passed = sem("p_passed")
            pad = sb("pad", [1, P], I32)
            given = sb("given", [SORT_T, 3, P], I32)
            givenf = sb("givenf", [SORT_T, 3, P])
            falls = sb("falls", [SORT_T, P])
            nfalls = sb("nfalls", [SORT_T, 1])
            ones = sb("ones", [P, 1])
            flag = sb("flag", [1, 1], I32)
            tri = sb("tri", [P, P])
            colf = sb("colf", [P, 2, SORT_T])
            coli = sb("coli", [P, 2, SORT_T], I32)
            bound = sb("bound", [P, SORT_T])
            row_i = sb("row_i", [P, NE], I32)
            vrow = sb("vrow", [P, SORT_T * P])
            junk = sb("junk", [P, SORT_T * P], BF16)
            tiejunk = sb("tiejunk", [P, P])
            less = sb("less", [P, SORT_T])
            ties = sb("ties", [P, SORT_T])
            rankf = sb("rankf", [P, SORT_T])
            ranki = sb("ranki", [P, SORT_T], I32)
            put_idx = sb("put_idx", [P, 1], I32)
            put_val = sb("put_val", [P, 2], I32)
            win = sb("win", [ET, 3, P], I32)
            winf = sb("winf", [ET, 3, P])
            wcol = sb("wcol", [P, 3, ET])
            same = sb("same", [P, ET])
            outf = sb("outf", [P, ET])
            dstf = sb("dstf", [P, ET])
            p_tr = ps("p_tr", [P, 3, P])
            p_cnt = ps("p_cnt", [1, 1])
            FULL, REST = E // P, E % P
            block = scope.enter_context(nc.Block())

            @block.sync
            def _(eng):
                eng.wait_ge(s_pad, 5)
                for j, (a, skip) in enumerate(((dst, 0), (dst, 1), (src, 0))):
                    whole, part = (E - skip) // P, (E - skip) % P
                    body = bass.AP(a.tensor, skip, [[P, whole], [1, P]])
                    eng.dma_start(given[0:whole, j, :], body).then_inc(s_in, 16)
                    if part:
                        rest = bass.AP(a.tensor, skip + whole * P, [[P, 1], [1, part]])
                        eng.dma_start(given[whole:whole + 1, j, 0:part], rest).then_inc(s_in, 16)
                cut = E // 8
                for table, a in ((edge_dst, dst), (edge_src, src)):
                    eng.dma_start(bass.AP(table.tensor, 1, [[cut, 8], [1, cut]]),
                                  bass.AP(a.tensor, 0, [[cut, 8], [1, cut]])).then_inc(s_fill, 16)
                eng.dma_start(bass.AP(edge_dst.tensor, 0, [[1, 1], [1, 1]]), pad[:, 0:1]).then_inc(s_fill, 16)
                eng.dma_start(bass.AP(edge_src.tensor, 0, [[1, 1], [1, 1]]), pad[:, 1:2]).then_inc(s_fill, 16)
                at = E + 1
                while at < NE:
                    w = min(60, NE - at)
                    eng.dma_start(bass.AP(edge_dst.tensor, at, [[w, 1], [1, w]]), pad[:, 2:2 + w]).then_inc(s_fill, 16)
                    eng.dma_start(bass.AP(edge_src.tensor, at, [[w, 1], [1, w]]), pad[:, 64:64 + w]).then_inc(s_fill, 16)
                    at += w
                fills = 4 + 2 * len(range(E + 1, NE, 60))
                eng.wait_ge(s_fill, 16 * fills)
                eng.wait_ge(s_flag, 1)
                unsorted = eng.value_load(flag[0:1, 0:1])
                with eng.If(unsorted > 0):
                    eng.dma_start(row_i[:, 0:E], replicated(dst, P, E)).then_inc(s_row, 16)
                eng.wait_ge(s_sorted, 1)
                for j, (table, ahead) in enumerate(((edge_dst, 0), (edge_dst, 1), (edge_src, 0))):
                    eng.dma_start(win[:, j, :], bass.AP(table.tensor, ahead, [[EPT, ET], [1, P]])).then_inc(s_win, 16)
                eng.dma_start(row_i[:, :], replicated(edge_dst, P, NE)).then_inc(s_key, 16)

            @block.gpsimd
            def _(eng):
                eng.memset(ident[:, :], 0.0).then_inc(s_const, 1)
                eng.memset(tri[:, :], 1.0).then_inc(s_const, 1)
                eng.memset(ones[:, :], 1.0).then_inc(s_const, 1)
                eng.wait_ge(s_const, 3)
                eng.affine_select(out=ident[:, :], in_=ident[:, :], compare_op=ALU.not_equal, fill=1.0, base=0,
                                  pattern=[[-1, P]], channel_multiplier=1).then_inc(s_const, 1)
                eng.affine_select(out=tri[:, :], in_=tri[:, :], compare_op=ALU.is_gt, fill=0.0, base=0,
                                  pattern=[[-1, P]], channel_multiplier=1).then_inc(s_const, 1)
                eng.wait_ge(s_const, 5)
                eng.tensor_copy(identb[:, :], ident[:, :]).then_inc(s_const, 1)
                fills = 4 + 2 * len(range(E + 1, NE, 60))
                eng.wait_ge(s_flag, 1)
                unsorted = eng.value_load(flag[0:1, 0:1])
                with eng.If(unsorted > 0):
                    eng.wait_ge(s_rank, 1)
                    eng.wait_ge(s_fill, 16 * fills)

                    def put(t):
                        wait(eng, s_put, t * 32)
                        eng.tensor_copy(put_idx[:, :], ranki[:, bass.ds(t, 1)]).then_inc(s_stage, 1)
                        eng.tensor_copy(put_val[:, 0:1], coli[:, 0, bass.ds(t, 1)]).then_inc(s_stage, 1)
                        eng.tensor_copy(put_val[:, 1:2], coli[:, 1, bass.ds(t, 1)]).then_inc(s_stage, 1)
                        wait_apart(eng, s_passed, (s_stage, t * 3 + 3))
                        for j, table in enumerate((edge_dst, edge_src)):
                            eng.indirect_dma_start(table, bass.IndirectOffsetOnAxis(ap=put_idx[:, 0:1], axis=0),
                                                   put_val[:, j:j + 1], None, bounds_check=NE - 1,
                                                   oob_is_err=False).then_inc(s_put, 16)

                    put(0)
                    with eng.Fori(1, SORT_T) as t:
                        put(t)
                    eng.wait_ge(s_put, SORT_T * 32)
                eng.wait_ge(s_fill, 16 * fills)
                eng.sem_inc(s_sorted, 1)

            @block.tensor
            def _(eng):
                eng.wait_ge(s_cnt, 3)
                eng.wait_ge(s_const, 5)
                eng.matmul(p_cnt[:, :], nfalls[:, :], ones[0:SORT_T, :], start=True, stop=True).then_inc(s_tr, 1)
                for j in (0, 2):
                    eng.transpose(p_tr[:, j, 0:SORT_T], givenf[:, j, :], ident[0:SORT_T, 0:SORT_T]).then_inc(s_tr, 1)
                eng.wait_ge(s_wf, 1)
                eng.wait_ge(s_col, 2)
                for j in range(3):
                    eng.transpose(p_tr[:, j, 0:ET], winf[:, j, :], ident[0:ET, 0:ET]).then_inc(s_wt, 1)

            @block.vector
            def _(eng):
                eng.memset(given[:, :, :], NO_NODE).then_inc(s_zero, 1)
                eng.memset(pad[:, :], NO_NODE).then_inc(s_zero, 1)
                eng.wait_ge(s_zero, 2)
                eng.memset(given[:, 2, :], 0).then_inc(s_pad, 1)
                eng.memset(pad[:, 0:1], OTHER_NODE).then_inc(s_pad, 1)
                eng.memset(pad[:, 1:2], 0).then_inc(s_pad, 1)
                eng.memset(pad[:, 64:P], 0).then_inc(s_pad, 1)
                eng.memset(vrow[:, :], 2.0 * NO_NODE + 1.0).then_inc(s_pad, 1)
                loads = sum(1 + ((E - skip) % P > 0) for skip in (0, 1, 0))
                eng.wait_ge(s_in, 16 * loads)
                eng.tensor_copy(givenf[:, :, :], given[:, :, :]).then_inc(s_cnt, 1)
                eng.wait_ge(s_cnt, 1)
                eng.tensor_tensor(falls[:, :], givenf[:, 0, :], givenf[:, 1, :], ALU.is_gt).then_inc(s_cnt, 1)
                eng.wait_ge(s_cnt, 2)
                eng.tensor_reduce(nfalls[:, :], falls[:, :], AX_X, ALU.add).then_inc(s_cnt, 1)
                eng.wait_ge(s_tr, 3)
                eng.tensor_copy(flag[:, :], p_cnt[:, :]).then_inc(s_flag, 1)
                for j in range(2):
                    eng.tensor_copy(colf[:, j, :], p_tr[:, 2 * j, 0:SORT_T]).then_inc(s_col, 1)
                eng.wait_ge(s_flag, 1)
                unsorted = eng.value_load(flag[0:1, 0:1])
                with eng.If(unsorted > 0):
                    eng.wait_ge(s_col, 2)
                    eng.tensor_copy(coli[:, :, :], colf[:, :, :]).then_inc(s_v, 1)
                    eng.tensor_scalar(bound[:, :], colf[:, 0, :], 2.0, 1.0, ALU.mult, ALU.add).then_inc(s_v, 1)
                    eng.wait_ge(s_row, 16)
                    eng.tensor_scalar(vrow[:, 0:E], row_i[:, 0:E], 2.0, 1.0, ALU.mult, ALU.add).then_inc(s_v, 1)
                    eng.wait_ge(s_v, 3)

                    def rank(t):
                        wait(eng, s_b, t * 2)
                        wait(eng, s_a, t)
                        eng.tensor_scalar(junk[:, :], vrow[:, :], bound[:, bass.ds(t, 1)], 0.0, ALU.is_lt, ALU.add,
                                          accum_out=less[:, bass.ds(t, 1)]).then_inc(s_a, 1)
                        eng.scalar_tensor_tensor(tiejunk[:, :], vrow[:, bass.ds(t * P, P)], bound[:, bass.ds(t, 1)],
                                                 tri[:, :], ALU.is_equal, ALU.mult,
                                                 accum_out=ties[:, bass.ds(t, 1)]).then_inc(s_b, 1)
                        eng.wait_ge(s_a, t + 1)
                        eng.wait_ge(s_b, t * 2 + 1)
                        eng.tensor_scalar(vrow[:, bass.ds(t * P, P)], vrow[:, bass.ds(t * P, P)], -1.0, None,
                                          ALU.add).then_inc(s_b, 1)

                    rank(0)
                    with eng.Fori(1, SORT_T) as t:
                        rank(t)
                    eng.wait_ge(s_b, 2 * SORT_T)
                    eng.scalar_tensor_tensor(rankf[:, :], less[:, :], 1.0, ties[:, :], ALU.add,
                                             ALU.add).then_inc(s_v, 1)
                    eng.wait_ge(s_v, 4)
                    eng.tensor_copy(ranki[:, :], rankf[:, :]).then_inc(s_rank, 1)
                eng.wait_ge(s_win, 48)
                eng.tensor_copy(winf[:, :, :], win[:, :, :]).then_inc(s_wf, 1)
                eng.wait_ge(s_wt, 3)
                eng.tensor_copy(wcol[:, :, :], p_tr[:, :, 0:ET]).then_inc(s_wc, 1)
                eng.wait_ge(s_wc, 1)
                eng.tensor_copy(key_col[:, :], wcol[:, 0, :]).then_inc(s_g, 1)
                eng.tensor_copy(src_idx[:, :], wcol[:, 2, :]).then_inc(s_g, 1)
                eng.tensor_scalar(dst_idx[:, :], wcol[:, 0, :], float(N - 1), None, ALU.min).then_inc(s_g, 1)
                eng.tensor_tensor(same[:, :], wcol[:, 0, :], wcol[:, 1, :], ALU.is_equal).then_inc(s_g, 1)
                eng.wait_ge(s_g, 4)
                eng.scalar_tensor_tensor(outf[:, :], same[:, :], float(OTHER_NODE), wcol[:, 0, :], ALU.mult,
                                         ALU.add).then_inc(s_g, 1)
                eng.wait_ge(s_g, 5)
                eng.tensor_copy(out_idx[:, :], outf[:, :]).then_inc(s_g, 1)
                eng.wait_ge(s_g, 6)
                eng.memset(out_idx[0:1, :], OTHER_NODE).then_inc(s_g, 1)
                eng.wait_ge(s_key, 16)
                eng.tensor_copy(key_row[:, :], row_i[:, :]).then_inc(s_g, 1)
                eng.wait_ge(s_g, 8)
                eng.memset(border[:, 0:1], FAR).then_inc(s_g, 1)
                eng.tensor_tensor(border[:, 1:NE], key_row[0:H, 1:NE], key_row[0:H, 0:NE - 1],
                                  ALU.not_equal).then_inc(s_g, 1)
                eng.wait_ge(s_g, 10)
                eng.tensor_scalar(border[:, 1:NE], border[:, 1:NE], FAR, None, ALU.mult).then_inc(s_g, 1)
                eng.wait_ge(s_g, 11)

        end_phase()

        with ExitStack() as scope:
            X = [sb(f"X{j}", [P, G, D]) for j in range(8)]
            A = [sb(f"A{j}", [P, G, D]) for j in range(4)]
            B = [sb(f"B{j}", [P, G, D]) for j in range(4)]
            norm_w = [sb(f"norm_w{j}", [P, D]) for j in range(3)]
            norm_b = [sb(f"norm_b{j}", [P, D]) for j in range(3)]
            stats = sb("stats", [P, 3, 2, G, 2, 6])
            mv = sb("mv", [P, 3, 2, G, 2])
            r = sb("r", [P, 3, 2, G])
            r0 = sb("r0", [P, 2, G])
            vr = sb("vr", [P, 2, G])
            nm = sb("nm", [P, 3, 2, G])
            power = sb("power", [P, G])
            s_vec, s_pow = sem("n_vec"), sem("n_pow")
            s_x = [sem(f"n_x{j}") for j in range(8)]
            s_hout = [sem(f"n_hout{j}") for j in range(4)]
            s_xout = [sem(f"n_xout{j}") for j in range(4)]
            s_bn, s_mv, s_rs, s_r, s_nm, s_z, s_w, s_y = ([sem(f"n_{n}{lv}") for lv in range(3)]
                                                        for n in ("bn", "mv", "rs", "r", "nm", "z", "w", "y"))
            s_x1, s_half = sem("n_sum"), sem("n_half")
            s_passed = sem("n_passed")
            block = scope.enter_context(nc.Block())
            source, target = (X, A, B), (A, B, B)

            def parts(b):
                return LAST // G if b.fixed and b.r == NB - 1 else P

            def node_rows(table, b):
                n = parts(b)
                return table[bass.ds(b.n * (P * G), n * G), :].rearrange("(p g) d -> p (g d)", g=G)

            @block.sync
            def _(eng):
                for j, v in enumerate((ln_w[0], ln_w[1], on_w)):
                    eng.dma_start(norm_w[j][:, :], replicated(v, P, D)).then_inc(s_vec, 16)
                for j, v in enumerate((ln_b[0], ln_b[1], on_b)):
                    eng.dma_start(norm_b[j][:, :], replicated(v, P, D)).then_inc(s_vec, 16)

                def body(i):
                    if (b := i.of(-1)).inside(NB):
                        eng.wait_ge(s_y[0], b.n + 1)
                        eng.dma_start(node_rows(h_table, b), A[b.slot(4)][0:parts(b), :, :].rearrange(
                            "p g d -> p (g d)")).then_inc(s_hout[b.slot(4)], 16)
                    if (b := i.of(-3)).inside(NB):
                        eng.wait_ge(s_x1, b.n + 1)
                        eng.dma_start(node_rows(x_table, b), B[b.slot(4)][0:parts(b), :, :].rearrange(
                            "p g d -> p (g d)")).then_inc(s_xout[b.slot(4)], 16)
                    if (b := i.of(2)).inside(NB):
                        wait(eng, s_x1, b.n - 7)
                        eng.dma_start(X[b.slot(8)][0:parts(b), :, :].rearrange("p g d -> p (g d)"),
                                      node_rows(x, b)).then_inc(s_x[b.slot(8)], 16)

                pipeline(eng, body, -2, NB, 2, 4, 8)
                for j in range(4):
                    uses = len(range(j, NB, 4))
                    eng.wait_ge(s_hout[j], 16 * uses)
                    eng.wait_ge(s_xout[j], 16 * uses)

            @block.vector
            def _(eng):
                def moments(lv, b):
                    c, q = b.slot(8 if lv == 0 else 4), b.slot(2)
                    wait(eng, s_nm[lv], b.n - 1)
                    for g in range(G):
                        for h in range(2):
                            op = eng.bn_stats(stats[:, lv, q, g, h, :], source[lv][c][:, g, h * HALF:(h + 1) * HALF])
                    op.then_inc(s_bn[lv], 1)
                    wait_apart(eng, s_passed, (s_bn[lv], b.n + 1))
                    for g in range(G):
                        op = eng.bn_aggr(mv[:, lv, q, g, :], stats[:, lv, q, g, :, :].rearrange("p a b -> p (a b)"))
                    op.then_inc(s_mv[lv], 1)

                def shift(lv, b):
                    eng.wait_ge(s_w[lv], b.n + 1)
                    t = target[lv][b.slot(4)]
                    if lv == 0:
                        q = b.slot(2)
                        eng.wait_ge(s_nm[0], b.n + 1)
                        eng.scalar_tensor_tensor(t[:, 0, :], X[b.slot(8)][:, 0, :], mv[:, 0, q, 0, 0:1],
                                                 norm_w[0][:, :], ALU.subtract, ALU.mult).then_inc(s_half, 1)
                        eng.tensor_tensor(t[:, 1:G, :], t[:, 1:G, :],
                                          norm_b[0][:, :].unsqueeze(1).broadcast_to([P, G - 1, D]), ALU.add)
                        eng.wait_ge(s_half, b.n + 1)
                        eng.scalar_tensor_tensor(t[:, 0, :], t[:, 0, :], r[:, 0, q, 0:1], norm_b[0][:, :],
                                                 ALU.mult, ALU.add).then_inc(s_y[0], 1)
                    else:
                        eng.tensor_tensor(t[:, :, :], t[:, :, :],
                                          norm_b[lv][:, :].unsqueeze(1).broadcast_to([P, G, D]),
                                          ALU.add).then_inc(s_y[lv], 1)

                def body(i):
                    if (b := i).inside(NB):
                        eng.wait_ge(s_x[b.slot(8)], b.turn(8) * 16 + 16)
                        moments(0, b)
                    if (b := i.of(-1)).inside(NB):
                        shift(0, b)
                        eng.wait_ge(s_y[0], b.n + 1)
                        moments(1, b)
                    if (b := i.of(-2)).inside(NB):
                        shift(1, b)
                        eng.wait_ge(s_y[1], b.n + 1)
                        moments(2, b)
                    if (b := i.of(-3)).inside(NB):
                        shift(2, b)
                        c = b.slot(4)
                        eng.wait_ge(s_y[2], b.n + 1)
                        eng.tensor_tensor(B[c][:, :, :], X[b.slot(8)][:, :, :], B[c][:, :, :], ALU.add).then_inc(s_x1, 1)

                eng.wait_ge(s_vec, 96)
                pipeline(eng, body, 0, NB, 2, 4, 8)

            @block.gpsimd
            def _(eng):
                eng.memset(power[:, :], -0.5).then_inc(s_pow, 1)
                eng.wait_ge(s_pow, 1)
                eng.wait_ge(s_vec, 96)

                def rstd(lv, b):
                    q = b.slot(2)
                    wait_apart(eng, s_passed, (s_mv[lv], b.n + 1), (s_z[lv], b.n - 1), (s_y[lv], b.n - 1))
                    eng.tensor_scalar(r[:, lv, q, :], mv[:, lv, q, :, 1], EPS, None, ALU.add).then_inc(s_rs[lv], 1)
                    n = b.n * (6 if lv == 0 else 2)
                    eng.wait_ge(s_rs[lv], n + 1)
                    eng.tensor_tensor(r[:, lv, q, :], r[:, lv, q, :], power[:, :], ALU.pow).then_inc(s_rs[lv], 1)
                    eng.wait_ge(s_rs[lv], n + 2)
                    if lv == 0:
                        eng.tensor_tensor(vr[:, q, :], r[:, 0, q, :], r[:, 0, q, :], ALU.mult).then_inc(s_rs[0], 1)
                        eng.wait_ge(s_rs[0], n + 3)
                        eng.tensor_tensor(vr[:, q, :], vr[:, q, :], mv[:, 0, q, :, 1], ALU.mult).then_inc(s_rs[0], 1)
                        wait_apart(eng, s_passed, (s_rs[0], n + 4))
                        eng.tensor_scalar(vr[:, q, :], vr[:, q, :], EPS, None, ALU.add).then_inc(s_rs[0], 1)
                        eng.wait_ge(s_rs[0], n + 5)
                        eng.tensor_tensor(vr[:, q, :], vr[:, q, :], power[:, :], ALU.pow).then_inc(s_rs[0], 1)
                        eng.wait_ge(s_rs[0], n + 6)
                        eng.tensor_tensor(r[:, 0, q, :], r[:, 0, q, :], vr[:, q, :], ALU.mult).then_inc(s_r[0], 1)
                        eng.wait_ge(s_r[0], b.n * 2 + 1)
                    eng.tensor_tensor(nm[:, lv, q, :], r[:, lv, q, :], mv[:, lv, q, :, 0], ALU.mult).then_inc(s_r[lv], 1)
                    wait_apart(eng, s_passed, (s_r[lv], b.n * (2 if lv == 0 else 1) + (2 if lv == 0 else 1)))
                    eng.tensor_scalar(nm[:, lv, q, :], nm[:, lv, q, :], -1.0, None, ALU.mult).then_inc(s_nm[lv], 1)

                def weigh(lv, b):
                    eng.wait_ge(s_z[lv], b.n + 1)
                    t = target[lv][b.slot(4)]
                    own = 1 if lv == 0 else 0
                    eng.tensor_tensor(t[:, own:G, :], t[:, own:G, :],
                                      norm_w[lv][:, :].unsqueeze(1).broadcast_to([P, G - own, D]),
                                      ALU.mult).then_inc(s_w[lv], 1)

                def body(i):
                    if (b := i).inside(NB):
                        rstd(0, b)
                    if (b := i.of(-3)).inside(NB):
                        weigh(2, b)
                    if (b := i.of(-1)).inside(NB):
                        rstd(1, b)
                    if (b := i).inside(NB):
                        weigh(0, b)
                    if (b := i.of(-2)).inside(NB):
                        rstd(2, b)
                    if (b := i.of(-1)).inside(NB):
                        weigh(1, b)

                pipeline(eng, body, 0, NB, 2, 4, 8)

            @block.scalar
            def _(eng):
                def normalise(lv, b):
                    c, q = b.slot(4), b.slot(2)
                    given = source[lv][b.slot(8 if lv == 0 else 4)]
                    eng.wait_ge(s_nm[lv], b.n + 1)
                    if lv == 0:
                        wait(eng, s_hout[c], b.turn(4) * 16)
                        wait(eng, s_z[1], b.n - 3)
                    if lv == 1:
                        wait(eng, s_xout[c], b.turn(4) * 16)
                    for g in range(1 if lv == 0 else 0, G):
                        op = eng.activation(target[lv][c][:, g, :], given[:, g, :], ACT.Identity,
                                            bias=nm[:, lv, q, g:g + 1], scale=r[:, lv, q, g:g + 1])
                    op.then_inc(s_z[lv], 1)

                def body(i):
                    if (b := i).inside(NB):
                        normalise(0, b)
                    if (b := i.of(-1)).inside(NB):
                        normalise(1, b)
                    if (b := i.of(-2)).inside(NB):
                        normalise(2, b)

                pipeline(eng, body, 0, NB, 2, 4, 8)

        end_phase()

        for layer in range(L):
            scope_ = ExitStack()
            with scope_:
                scope = scope_
                edge_layer(nc, sb, ps, sem, scope, layer, layer == L - 1,
                           dict(N=N, D=D, H=H, HD=HD, KC=KC, HALF=HALF, EPT=EPT, ET=ET, ident=ident, key_row=key_row,
                                border=border, key_col=key_col, src_idx=src_idx, dst_idx=dst_idx, out_idx=out_idx),
                           x if layer == 0 else h_table, x, Wsrc[layer], bsrc[layer], Wdst[layer], bdst[layer],
                           attn[layer].rearrange("h d -> (h d)"), ln_w[layer], ln_b[layer], on_w, on_b,
                           x_table if layer == L - 1 else h_table)
            end_phase()

        with ExitStack() as scope:
            NT = G * P
            X = [sb(f"fX{j}", [P, G, D]) for j in range(8)]
            Y = [sb(f"fY{j}", [P, G, D]) for j in range(2)]
            XQ = [sb(f"fXQ{j}", [P, G, D], BF16) for j in range(2)]
            XT = [sb(f"fXT{j}", [P, KC, NT], BF16) for j in range(2)]
            HG = [sb(f"fHG{j}", [F, NT]) for j in range(2)]
            HQ = [sb(f"fHQ{j}", [65, NT], BF16) for j in range(2)]
            stats = sb("f_stats", [P, 2, G, 2, 6])
            mv = sb("f_mv", [P, 2, G, 2])
            r = sb("f_r", [P, 2, G])
            nm = sb("f_nm", [P, 2, G])
            OC = [sb(f"fOC{j}", [P, G, D]) for j in range(2)]
            power = sb("f_power", [P, G])
            w1_in, w1_q, w1_b = sb("w1_in", [F, D]), sb("w1_q", [F, D]), sb("w1_b", [F, D], BF16)
            w1T = sb("w1T", [P, KC, F], BF16)
            w2_in, w2_q = sb("w2_in", [P, KC, F]), sb("w2_q", [P, KC, F])
            w2T, w2rest = sb("w2T", [65, D]), sb("w2rest", [65, D])
            w2p = sb("w2p", [65, 3, D], BF16)
            a1_row, a2_row = sb("a1_row", [P, D]), sb("a2_row", [F, F])
            a2_all = sb("a2_all", [P, F])
            step1 = sb("step1", [P, 2])
            step2 = sb("step2", [P, 2])
            aw1, b1c = sb("aw1", [F, 2]), sb("b1c", [F, 2])
            aw2 = sb("aw2", [P, KC, 2])
            pT = ps("fpT", [P, 2, 1024], BF16)
            pH = ps("fpH", [F, 512])
            pO = ps("fpO", [P, G, 2, 512])
            s_c = sem("f_c")
            s_passed = sem("f_passed")
            s_pow = sem("f_pow")
            s_cd, s_ct, s_ca, s_setup = sem("f_cd"), sem("f_ct"), sem("f_ca"), sem("f_setup")
            s_x = [sem(f"f_x{j}") for j in range(8)]
            s_out = [sem(f"f_out{j}") for j in range(8)]
            (s_bn, s_mv, s_ra, s_rb, s_r, s_y, s_clip, s_q, s_tr, s_xt, s_hid, s_gelu, s_h1, s_h2, s_h3, s_hq, s_o,
             s_fin) = (sem(f"f_{n}") for n in ("bn", "mv", "ra", "rb", "r", "y", "clip", "q", "tr", "xt", "hid",
                                               "gelu", "h1", "h2", "h3", "hq", "o", "fin"))
            s_oc, s_nm0, s_nm = sem("f_oc"), sem("f_nm0"), sem("f_nm")
            block = scope.enter_context(nc.Block())

            @block.sync
            def _(eng):
                eng.wait_ge(s_pow, 4)
                for t, v in ((w1_in[:, :], w1), (w2_in[:, :, :], w2.rearrange("(c p) f -> p c f", p=P)),
                             (a1_row[:, :], replicated(alpha_a1, P, D)), (a2_all[:, :], replicated(alpha_a2, P, F)),
                             (aw1[:, 0:1], alpha_w1.unsqueeze(1)), (b1c[:, 0:1], b1.unsqueeze(1)),
                             (w2T[64:65, :], b2.unsqueeze(0))):
                    eng.dma_start(t, v).then_inc(s_c, 16)
                eng.dma_start(aw2[:, :, 0], alpha_w2.rearrange("(c p) -> p c", p=P),
                              allow_slow_non_contiguous=True).then_inc(s_c, 16)

                def body(i):
                    if (b := i.of(3)).inside(NB):
                        wait(eng, s_out[b.slot(8)], b.turn(8) * 16)
                        eng.dma_start(X[b.slot(8)][0:parts(b), :, :].rearrange("p g d -> p (g d)"),
                                      node_rows(x_table, b)).then_inc(s_x[b.slot(8)], 16)
                    if (b := i.of(-3)).inside(NB):
                        eng.wait_ge(s_fin, b.n + 1)
                        eng.dma_start(node_rows(out, b), X[b.slot(8)][0:parts(b), :, :].rearrange(
                            "p g d -> p (g d)")).then_inc(s_out[b.slot(8)], 16)

                pipeline(eng, body, -3, NB, 3, 4, 8)
                for j in range(8):
                    eng.wait_ge(s_out[j], 16 * len(range(j, NB, 8)))

            @block.gpsimd
            def _(eng):
                eng.memset(power[:, :], -0.5).then_inc(s_pow, 1)
                eng.memset(w2T[:, :], 0.0).then_inc(s_pow, 1)
                for j in range(2):
                    eng.memset(HQ[j][:, :], 0.0).then_inc(s_pow, 1)
                eng.wait_ge(s_pow, 4)
                for j in range(2):
                    eng.memset(HQ[j][64:65, :], 1.0).then_inc(s_pow, 1)
                eng.wait_ge(s_setup, 1)

                def body(i):
                    if (b := i.of(1)).inside(NB):
                        q = b.slot(2)
                        wait_apart(eng, s_passed, (s_mv, b.n + 1), (s_y, b.n - 1))
                        eng.tensor_scalar(r[:, q, :], mv[:, q, :, 1], EPS, None, ALU.add).then_inc(s_ra, 1)
                        eng.wait_ge(s_ra, b.n + 1)
                        eng.tensor_tensor(r[:, q, :], r[:, q, :], power[:, :], ALU.pow).then_inc(s_rb, 1)
                        wait_apart(eng, s_passed, (s_rb, b.n + 1))
                        eng.tensor_scalar(r[:, q, :], r[:, q, :], step1[:, 1:2], None, ALU.mult).then_inc(s_r, 1)
                        eng.wait_ge(s_r, b.n + 1)
                        eng.tensor_tensor(nm[:, q, :], mv[:, q, :, 0], r[:, q, :], ALU.mult).then_inc(s_nm0, 1)
                        wait_apart(eng, s_passed, (s_nm0, b.n + 1))
                        eng.tensor_scalar(nm[:, q, :], nm[:, q, :], -1.0, None, ALU.mult).then_inc(s_nm, 1)
                    if (b := i.of(-3)).inside(NB):
                        xb = X[b.slot(8)]
                        eng.wait_ge(s_oc, b.n + 1)
                        eng.tensor_tensor(xb[:, :, :], OC[b.slot(2)][:, :, :], xb[:, :, :], ALU.add).then_inc(s_fin, 1)

                pipeline(eng, body, -1, NB, 3, 4, 8)

            @block.tensor
            def _(eng):
                eng.wait_ge(s_cd, 11)
                for c in range(KC):
                    op = eng.transpose(pT[:, 0, c * 64:c * 64 + F], w1_b[:, c * P:(c + 1) * P], identb[0:F, 0:F])
                op.then_inc(s_ct, 1)
                eng.wait_ge(s_cd, 16)
                for c in range(KC):
                    op = eng.transpose(pO[0:F, 0, c // 3, (c % 3) * P:(c % 3 + 1) * P], w2_q[:, c, :], ident[:, :])
                op.then_inc(s_ct, 1)

                def body(i):
                    if (b := i).inside(NB):
                        q = b.slot(2)
                        eng.wait_ge(s_q, b.n + 1)
                        if b.fixed and b.r == 0:
                            eng.wait_ge(s_ca, 2)
                        wait(eng, s_xt, b.n)
                        for c in range(KC):
                            for g in range(G):
                                at = (c % 3) * NT + g * P
                                op = eng.transpose(pT[:, c // 3, at:at + P], XQ[q][:, g, c * P:(c + 1) * P],
                                                   identb[:, :])
                        op.then_inc(s_tr, 1)
                    if (b := i.of(-2)).inside(NB):
                        q = b.slot(2)
                        eng.wait_ge(s_hq, b.n + 1)
                        wait(eng, s_oc, b.n)
                        for g in range(G):
                            for h in range(2):
                                for part in range(3):
                                    op = eng.matmul(pO[:, g, h, 0:HALF], HQ[q][:, g * P:(g + 1) * P],
                                                    w2p[:, part, h * HALF:(h + 1) * HALF], start=part == 0,
                                                    stop=part == 2)
                        op.then_inc(s_o, 1)
                    if (b := i).inside(NB):
                        q = b.slot(2)
                        eng.wait_ge(s_xt, b.n + 1)
                        wait(eng, s_gelu, b.n)
                        for c in range(KC):
                            op = eng.matmul(pH[:, 0:NT], w1T[:, c, :], XT[q][:, c, :], start=c == 0,
                                            stop=c == KC - 1)
                        op.then_inc(s_hid, 1)

                pipeline(eng, body, 0, NB, 3, 4, 8)

            @block.scalar
            def _(eng):
                eng.wait_ge(s_ct, 1)
                eng.activation(w1T[:, :, :], pT[:, 0, 0:KC * 64].rearrange("p (c f) -> p c f", f=64)[:, :, 0:F],
                               ACT.Copy).then_inc(s_ca, 1)
                eng.wait_ge(s_ct, 2)
                eng.activation(w2T[0:F, :].rearrange("p (h d) -> p h d", h=2), pO[0:F, 0, :, 0:HALF],
                               ACT.Copy).then_inc(s_ca, 1)

                eng.wait_ge(s_setup, 1)

                def normalise(b):
                    q = b.slot(2)
                    eng.wait_ge(s_nm, b.n + 1)
                    wait(eng, s_q, b.n - 1)
                    for g in range(G):
                        op = eng.activation(Y[q][:, g, :], X[b.slot(8)][:, g, :], ACT.Identity,
                                            bias=nm[:, q, g:g + 1], scale=r[:, q, g:g + 1])
                    op.then_inc(s_y, 1)

                def body(i):
                    if (b := i).inside(NB):
                        q = b.slot(2)
                        eng.wait_ge(s_tr, b.n + 1)
                        wait(eng, s_hid, b.n - 1)
                        for h in range(2):
                            op = eng.activation(XT[q][:, 3 * h:3 * h + 3, :].rearrange("p c n -> p (c n)"),
                                                pT[:, h, 0:3 * NT], ACT.Copy)
                        op.then_inc(s_xt, 1)
                    if (b := i.of(1)).inside(NB):
                        normalise(b)
                    if (b := i.of(-2)).inside(NB):
                        q = b.slot(2)
                        eng.wait_ge(s_o, b.n + 1)
                        wait(eng, s_fin, b.n - 1)
                        for g in range(G):
                            op = eng.activation(OC[q][:, g, :].rearrange("p (h d) -> p h d", h=2), pO[:, g, :, 0:HALF],
                                                ACT.Copy)
                        op.then_inc(s_oc, 1)
                    if (b := i).inside(NB):
                        q = b.slot(2)
                        eng.wait_ge(s_hid, b.n + 1)
                        wait(eng, s_h1, b.n - 1)
                        eng.activation(HG[q][:, :], pH[:, 0:NT], ACT.Gelu, bias=b1c[:, 0:1],
                                       scale=aw1[:, 1:2]).then_inc(s_gelu, 1)

                pipeline(eng, body, -1, NB, 3, 4, 8)

            @block.vector
            def _(eng):
                eng.wait_ge(s_c, 128)

                def link(op):
                    op.then_inc(s_cd, 1)

                link(eng.tensor_reduce(step1[:, 0:1], a1_row[:, :], AX_X, ALU.add))
                link(eng.tensor_reduce(step2[:, 0:1], a2_all[:, :], AX_X, ALU.add))
                eng.wait_ge(s_cd, 2)
                link(eng.tensor_scalar(step1[:, 0:1], step1[:, 0:1], 1.0 / D, None, ALU.mult))
                link(eng.tensor_scalar(step2[:, 0:1], step2[:, 0:1], 1.0 / F, None, ALU.mult))
                eng.wait_ge(s_cd, 4)
                link(eng.reciprocal(step1[:, 1:2], step1[:, 0:1]))
                link(eng.reciprocal(step2[:, 1:2], step2[:, 0:1]))
                link(eng.reciprocal(b1c[:, 1:2], aw1[:, 0:1]))
                eng.wait_ge(s_cd, 7)
                link(eng.tensor_scalar(w1_q[:, :], w1_in[:, :], b1c[:, 1:2], QN, ALU.mult, ALU.max))
                eng.wait_ge(s_cd, 8)
                link(eng.tensor_scalar(w1_q[:, :], w1_q[:, :], QP, ROUND, ALU.min, ALU.add))
                eng.wait_ge(s_cd, 9)
                link(eng.tensor_scalar(w1_b[:, :], w1_q[:, :], -ROUND, None, ALU.add))
                link(eng.tensor_tensor(aw1[:, 1:2], aw1[:, 0:1], step1[0:F, 0:1], ALU.mult))
                link(eng.reciprocal(aw2[:, :, 1], aw2[:, :, 0]))
                eng.wait_ge(s_cd, 12)
                link(eng.tensor_tensor(w2_q[:, :, :], w2_in[:, :, :],
                                       aw2[:, :, 1:2].broadcast_to([P, KC, F]), ALU.mult))
                eng.wait_ge(s_cd, 13)
                link(eng.tensor_scalar(w2_q[:, :, :], w2_q[:, :, :], QN, QP, ALU.max, ALU.min))
                eng.wait_ge(s_cd, 14)
                link(eng.tensor_scalar(w2_q[:, :, :], w2_q[:, :, :], ROUND, -ROUND, ALU.add, ALU.add))
                eng.wait_ge(s_cd, 15)
                link(eng.tensor_tensor(w2_q[:, :, :], w2_q[:, :, :],
                                       aw2[:, :, 0:1].broadcast_to([P, KC, F]), ALU.mult))
                eng.wait_ge(s_ca, 2)
                link(eng.tensor_scalar(w2T[0:F, :], w2T[0:F, :], step2[0:F, 0:1], None, ALU.mult))
                eng.wait_ge(s_cd, 17)
                link(eng.tensor_copy(w2p[:, 0, :], w2T[:, :]))
                eng.wait_ge(s_cd, 18)
                link(eng.tensor_tensor(w2rest[:, :], w2T[:, :], w2p[:, 0, :], ALU.subtract))
                eng.wait_ge(s_cd, 19)
                link(eng.tensor_copy(w2p[:, 1, :], w2rest[:, :]))
                eng.wait_ge(s_cd, 20)
                link(eng.tensor_tensor(w2p[:, 2, :], w2rest[:, :], w2p[:, 1, :], ALU.subtract))
                eng.wait_ge(s_cd, 21)
                eng.wait_ge(s_pow, 6)
                eng.sem_inc(s_setup, 1)

                def body(i):
                    if (b := i.of(1)).inside(NB):
                        c, q = b.slot(8), b.slot(2)
                        eng.wait_ge(s_x[c], b.turn(8) * 16 + 16)
                        wait(eng, s_nm0, b.n - 1)
                        for g in range(G):
                            for h in range(2):
                                op = eng.bn_stats(stats[:, q, g, h, :], X[c][:, g, h * HALF:(h + 1) * HALF])
                        op.then_inc(s_bn, 1)
                        wait_apart(eng, s_passed, (s_bn, b.n + 1))
                        for g in range(G):
                            op = eng.bn_aggr(mv[:, q, g, :], stats[:, q, g, :, :].rearrange("p a b -> p (a b)"))
                        op.then_inc(s_mv, 1)
                    if (b := i).inside(NB):
                        c, q = b.slot(8), b.slot(2)
                        eng.wait_ge(s_y, b.n + 1)
                        eng.tensor_scalar(Y[q][:, :, :], Y[q][:, :, :], QN, QP, ALU.max, ALU.min).then_inc(s_clip, 1)
                        eng.wait_ge(s_clip, b.n + 1)
                        wait(eng, s_tr, b.n - 1)
                        eng.tensor_scalar(XQ[q][:, :, :], Y[q][:, :, :], ROUND, -ROUND, ALU.add,
                                          ALU.add).then_inc(s_q, 1)
                    if (b := i.of(-1)).inside(NB):
                        q = b.slot(2)
                        eng.wait_ge(s_gelu, b.n + 1)
                        eng.tensor_scalar(HG[q][:, :], HG[q][:, :], -10.0, 10.0, ALU.max, ALU.min).then_inc(s_h2, 1)
                        eng.wait_ge(s_h2, b.n * 2 + 1)
                        eng.tensor_scalar(HG[q][:, :], HG[q][:, :], step2[0:F, 1:2], QN, ALU.mult,
                                          ALU.max).then_inc(s_h2, 1)
                        eng.wait_ge(s_h2, b.n * 2 + 2)
                        eng.tensor_scalar(HG[q][:, :], HG[q][:, :], QP, ROUND, ALU.min, ALU.add).then_inc(s_h3, 1)
                        eng.wait_ge(s_h3, b.n + 1)
                        wait(eng, s_o, b.n - 1)
                        eng.tensor_scalar(HQ[q][0:F, :], HG[q][:, :], -ROUND, None, ALU.add).then_inc(s_h1, 1)
                        eng.wait_ge(s_h1, b.n + 1)
                        eng.sem_inc(s_hq, 1)

                pipeline(eng, body, -1, NB, 3, 4, 8)


def edge_layer(nc, sb, ps, sem, scope, layer, final, s, h_in, x_in, Ws, bs, Wd, bd, attn, norm_w, norm_b, outer_w,
               outer_b, table):
    N, D, H, HD, KC, HALF, EPT, ET = (s[n] for n in ("N", "D", "H", "HD", "KC", "HALF", "EPT", "ET"))
    ident, key_row, border, key_col = s["ident"], s["key_row"], s["border"], s["key_col"]
    src_idx, dst_idx, out_idx = s["src_idx"], s["dst_idx"], s["out_idx"]
    first = layer == 0
    V = D + H
    LEAD, TAIL = 2, 6

    def name(x):
        return f"L{layer}_{x}"

    XS = [sb(name(f"XS{j}"), [P, D]) for j in range(2)]
    XD = [sb(name(f"XD{j}"), [P, D]) for j in range(4)]
    XR = [sb(name(f"XR{j}"), [P, D]) for j in range(2)] if final else None
    hT = [[sb(name(f"hT{side}{part}"), [P, D], F16) for part in range(2)] for side in range(2)]
    HS = [sb(name(f"HS{j}"), [P, V]) for j in range(4)]
    ZC = [sb(name(f"ZC{j}"), [P, D]) for j in range(2)]
    GA = [sb(name(f"GA{j}"), [P, D]) for j in range(2)]
    EX = [sb(name(f"EX{j}"), [P, D]) for j in range(2)]
    U = [sb(name(f"U{j}"), [P, D]) for j in range(4)]
    W = [[sb(name(f"W{side}{part}"), [P, KC, D], F16) for part in range(2)] for side in range(2)]
    STAGES = 3
    stage = [sb(name(f"stage{j}"), [P, D]) for j in range(STAGES)]
    bias_in = sb(name("bias_in"), [1, 2, D])
    bias_row = sb(name("bias_row"), [1, 2, 3, D], BF16)
    bias = sb(name("bias"), [3, 2, D], BF16)
    ones3 = sb(name("ones3"), [3, P], BF16)
    zero_row = sb(name("zero_row"), [1, D])
    attn_v, w_v, b_v = sb(name("attn_v"), [P, D]), sb(name("w_v"), [P, D]), sb(name("b_v"), [P, D])
    ow_v, ob_v = (sb(name("ow_v"), [P, D]), sb(name("ob_v"), [P, D])) if final else (None, None)
    idx_s, idx_d, idx_o = sb(name("idx_s"), [P, 2], I32), sb(name("idx_d"), [P, 4], I32), sb(name("idx_o"), [P, 4], I32)
    idx_r = sb(name("idx_r"), [P, 2], I32)
    M = [sb(name(f"M{j}"), [P, P]) for j in range(2)]
    Lg = sb(name("Lg"), [P, 2, H])
    LT = sb(name("LT"), [H, 2, P])
    scan = sb(name("scan"), [H, 2, 2, P])
    dif = sb(name("dif"), [H, 2, P])
    ahead = sb(name("ahead"), [H, 2, P])
    ex = sb(name("ex"), [H, 2, P])
    srow = sb(name("srow"), [1, 2, H])
    rs = sb(name("rs"), [P, 2, H])
    st = sb(name("st"), [P, 4, 2, 2, 6])
    mv = sb(name("mv"), [P, 4, 2, 2])
    rr = sb(name("rr"), [P, 4, 2])
    nm = sb(name("nm"), [P, 4, 2])
    power = sb(name("power"), [P, 1])
    pZ = ps(name("pZ"), [P, 2, 512])
    pT = ps(name("pT"), [P, 2, 512])
    pA = ps(name("pA"), [P, 2, 512])
    pS = ps(name("pS"), [P, 2, 512])
    VH = V // 2

    one = lambda n: sem(name(n))
    s_vec, s_const, s_whi, s_wlo, s_bias, s_brest, s_bplace = (one(n) for n in (
        "vec", "const", "whi", "wlo", "bias", "brest", "bplace"))
    s_wload = [one(f"wload{j}") for j in range(STAGES)]
    s_is, s_id, s_io, s_ir = one("is"), one("id"), one("io"), one("ir")
    s_ahead, s_passed = one("ahead"), one("passed")
    s_xs, s_xr = [one(f"xs{j}") for j in range(2)], [one(f"xr{j}") for j in range(2)]
    s_xd = [one(f"xd{j}") for j in range(4)]
    s_carry = [one(f"carry{j}") for j in range(4)]
    s_put = [one(f"put{j}") for j in range(4)]
    KIND = ("src", "dst", "u", "y")
    s_bn, s_mv, s_ra, s_rb, s_nm0, s_nm, s_nrm = ([one(f"{n}_{k}") for k in KIND] for n in (
        "bn", "mv", "ra", "rb", "nm0", "nm", "nrm"))
    s_tr, s_hi, s_lo = ([one(f"{n}{side}") for side in range(2)] for n in ("tr", "hi", "lo"))
    (s_hs, s_hscopy, s_z, s_zc, s_lrelu, s_att, s_logit, s_lt, s_ltc, s_fwd, s_max, s_dif, s_ex, s_wt, s_wc, s_w0,
     s_wv, s_m0, s_m, s_agg, s_srow, s_rs, s_ga, s_e, s_u0, s_u, s_yw, s_y, s_ow, s_ob, s_x1) = (one(n) for n in (
        "hs", "hscopy", "z", "zc", "lrelu", "att", "logit", "lt", "ltc", "fwd", "max", "dif", "ex", "wt", "wc", "w0",
        "wv", "m0", "m", "agg", "srow", "rs", "ga", "e", "u0", "u", "yw", "y", "ow", "ob", "x1"))
    block = scope.enter_context(nc.Block())
    pieces = [(w, side, c) for side, w in enumerate((Ws, Wd)) for c in range(KC)]
    KH = KC // 2

    @block.sync
    def _(eng):
        vectors = [(attn_v, attn), (w_v, norm_w), (b_v, norm_b)] + ([(ow_v, outer_w), (ob_v, outer_b)] if final else [])
        for t, v in vectors:
            eng.dma_start(t[:, :], replicated(v, P, D)).then_inc(s_vec, 16)
        for side, v in enumerate((bs, bd)):
            eng.dma_start(bias_in[:, side, :], v.unsqueeze(0)).then_inc(s_vec, 16)
        for n, (w, side, c) in enumerate(pieces):
            wait(eng, s_wlo, n + 1 - STAGES)
            eng.dma_start(stage[n % STAGES][:, :], w[c * P:(c + 1) * P, :]).then_inc(s_wload[n % STAGES], 16)
        eng.wait_ge(s_bias, 6)
        for side in range(2):
            for part in range(3):
                eng.dma_start(bias[part:part + 1, side, :], bias_row[:, side, part, :]).then_inc(s_bplace, 16)
        eng.wait_ge(s_const, 8)

        def body(i):
            if (t := i.of(-1)).inside(ET):
                wait_apart(eng, s_passed, (s_hscopy, t.n * 2 + 2))
                if t.fixed and t.r == 0:
                    eng.dma_start(HS[0][0:1, 0:D], zero_row[:, :]).then_inc(s_carry[0], 16)
                else:
                    eng.wait_ge(s_ga, t.n)
                    eng.dma_start(HS[t.slot(4)][0:1, 0:D], GA[(t.r - 1) % 2][0:1, :]).then_inc(
                        s_carry[t.slot(4)], 16)

        pipeline(eng, body, 0, ET, LEAD, TAIL)

    @block.gpsimd
    def _(eng):
        eng.memset(power[:, :], -0.5).then_inc(s_const, 1)
        eng.memset(ones3[:, :], 1.0).then_inc(s_const, 1)
        eng.memset(zero_row[:, :], 0.0).then_inc(s_const, 1)
        eng.memset(srow[:, :, :], 0.0).then_inc(s_const, 1)
        eng.memset(LT[:, :, :], 0.0).then_inc(s_const, 1)
        for j in range(2):
            eng.memset(ex[:, j, :], 0.0).then_inc(s_const, 1)
        eng.memset(Lg[:, :, :], 0.0).then_inc(s_const, 1)
        eng.wait_ge(s_const, 8)
        n_vec = 16 * (7 if final else 5)
        eng.wait_ge(s_vec, n_vec)

        def gather(idx, column, t, slots, source, sem_idx, done, target):
            eng.tensor_copy(idx[:, t.slot(slots):t.slot(slots) + 1], column[:, bass.ds(t.n, 1)]).then_inc(sem_idx, 1)
            wait_apart(eng, s_passed, (sem_idx, t.n + 1))
            eng.indirect_dma_start(target[t.slot(slots)][:, :], None, source, bass.IndirectOffsetOnAxis(
                ap=idx[:, t.slot(slots):t.slot(slots) + 1], axis=0), bounds_check=N - 1,
                oob_is_err=False).then_inc(done[t.slot(slots)], 16)

        def rstd(kind, t):
            q = t.slot(2)
            wait_apart(eng, s_passed, (s_mv[kind], t.n + 1), (s_nrm[kind], t.n - 1))
            eng.tensor_scalar(rr[:, kind, q:q + 1], mv[:, kind, q, 1:2], EPS, None, ALU.add).then_inc(s_ra[kind], 1)
            eng.wait_ge(s_ra[kind], t.n + 1)
            eng.tensor_tensor(rr[:, kind, q:q + 1], rr[:, kind, q:q + 1], power[:, :], ALU.pow).then_inc(s_rb[kind], 1)
            if kind >= 2:
                eng.wait_ge(s_rb[kind], t.n + 1)
                eng.tensor_tensor(nm[:, kind, q:q + 1], mv[:, kind, q, 0:1], rr[:, kind, q:q + 1], ALU.mult).then_inc(
                    s_nm0[kind], 1)
                wait_apart(eng, s_passed, (s_nm0[kind], t.n + 1))
                eng.tensor_scalar(nm[:, kind, q:q + 1], nm[:, kind, q:q + 1], -1.0, None, ALU.mult).then_inc(
                    s_nm[kind], 1)

        def body(i):
            if (t := i.of(-1)).inside(ET):
                eng.wait_ge(s_lrelu, t.n + 1)
                z = ZC[t.slot(2)]
                eng.tensor_tensor(z[:, :], z[:, :], attn_v[:, :], ALU.mult).then_inc(s_att, 1)
            if (t := i.of(1)).inside(ET) and first:
                rstd(0, t)
            if (t := i.of(2)).inside(ET):
                wait(eng, s_tr[0], t.n - 1)
                gather(idx_s, src_idx, t, 2, h_in, s_is, s_xs, XS)
            if (t := i.of(-4)).inside(ET):
                eng.wait_ge(s_nrm[2], t.n + 1)
                u = U[t.slot(4)]
                eng.tensor_tensor(u[:, :], u[:, :], w_v[:, :], ALU.mult).then_inc(s_yw, 1)
            if (t := i.of(1)).inside(ET):
                wait(eng, s_u0, t.n - 3)
                wait(eng, s_tr[1], t.n - 3)
                gather(idx_d, dst_idx, t, 4, h_in, s_id, s_xd, XD)
            if (t := i.of(-5)).inside(ET) and final:
                eng.wait_ge(s_nrm[3], t.n + 1)
                u = U[t.slot(4)]
                eng.tensor_tensor(u[:, :], u[:, :], ow_v[:, :], ALU.mult).then_inc(s_ow, 1)
            if (t := i.of(-3)).inside(ET):
                rstd(2, t)
            if (t := i.of(1)).inside(ET) and first:
                rstd(1, t)
            if (t := i.of(-4)).inside(ET) and final:
                wait(eng, s_x1, t.n - 1)
                gather(idx_r, dst_idx, t, 2, x_in, s_ir, s_xr, XR)
                rstd(3, t)
            if (t := i.of(-5)).inside(ET):
                c = t.slot(4)
                eng.tensor_copy(idx_o[:, c:c + 1], out_idx[:, bass.ds(t.n, 1)]).then_inc(s_io, 1)
                wait_apart(eng, s_passed, (s_io, t.n + 1), (s_x1 if final else s_y, t.n + 1))
                eng.indirect_dma_start(table, bass.IndirectOffsetOnAxis(ap=idx_o[:, c:c + 1], axis=0), U[c][:, :],
                                       None, bounds_check=N - 1, oob_is_err=False).then_inc(s_put[c], 16)

        pipeline(eng, body, -2, ET, LEAD, TAIL)
        for j in range(4):
            eng.wait_ge(s_put[j], 16 * len(range(j, ET, 4)))

    @block.tensor
    def _(eng):
        eng.wait_ge(s_wlo, len(pieces))
        eng.wait_ge(s_bplace, 96)
        eng.wait_ge(s_const, 8)

        def product(side, h, start):
            eng.matmul(pZ[:, h, 0:HALF], ones3[:, :], bias[:, side, h * HALF:(h + 1) * HALF], start=start,
                       stop=False, skip_group_check=True)
            for c in range(KC):
                for part, wpart in ((0, 0), (0, 1), (1, 0)):
                    op = eng.matmul(pZ[:, h, 0:HALF], hT[side][part][:, c * P:(c + 1) * P],
                                    W[side][wpart][:, c, h * HALF:(h + 1) * HALF], start=False,
                                    stop=c == KC - 1 and part == 1, skip_group_check=True)
            return op

        def transposes(side, t):
            eng.wait_ge(s_nrm[side] if first else (s_xs[t.slot(2)] if side == 0 else s_xd[t.slot(4)]),
                        t.n + 1 if first else (t.turn(2) * 16 + 16 if side == 0 else t.turn(4) * 16 + 16))
            wait(eng, s_lo[1 - side], t.n if side == 0 else t.n + 1)
            rows_in = XS[t.slot(2)] if side == 0 else XD[t.slot(4)]
            for c in range(KC):
                op = eng.transpose(pT[:, c // KH, (c % KH) * P:(c % KH + 1) * P], rows_in[:, c * P:(c + 1) * P],
                                   ident[:, :])
            op.then_inc(s_tr[side], 1)

        def body(i):
            if (t := i).inside(ET):
                eng.wait_ge(s_lo[0], t.n + 1)
                for h in range(2):
                    wait(eng, s_zc, t.n * 2 + (h - 1))
                    product(0, h, True).then_inc(s_hs, 1)
            if (t := i.of(1)).inside(ET):
                transposes(0, t)
            if (t := i.of(-2)).inside(ET):
                eng.wait_ge(s_wv, t.n + 1)
                eng.wait_ge(s_m, t.n + 1)
                wait(eng, s_ga, t.n)
                for h in range(2):
                    op = eng.matmul(pA[:, h, 0:VH], M[t.slot(2)][:, :], HS[t.slot(4)][:, h * VH:(h + 1) * VH],
                                    start=True, stop=True)
                op.then_inc(s_agg, 1)
            if (t := i.of(-1)).inside(ET):
                eng.wait_ge(s_logit, t.n + 1)
                wait(eng, s_ltc, t.n)
                eng.transpose(pS[0:H, 0, 0:P], Lg[:, t.slot(2), :], ident[:, :]).then_inc(s_lt, 1)
            if (t := i).inside(ET):
                eng.wait_ge(s_lo[1], t.n + 1)
                for h in range(2):
                    eng.wait_ge(s_hscopy, t.n * 2 + (h + 1))
                    product(1, h, False).then_inc(s_z, 1)
            if (t := i.of(1)).inside(ET):
                transposes(1, t)
            if (t := i.of(-1)).inside(ET):
                wait_apart(eng, s_passed, (s_ex, t.n + 1), (s_wc, t.n))
                eng.transpose(pS[:, 1, 0:H], ex[:, t.slot(2), :], ident[0:H, 0:H]).then_inc(s_wt, 1)

        pipeline(eng, body, -1, ET, LEAD, TAIL)

    @block.scalar
    def _(eng):
        for n, (w, side, c) in enumerate(pieces):
            eng.wait_ge(s_wload[n % STAGES], 16 * (n // STAGES) + 16)
            eng.activation(W[side][0][:, c, :], stage[n % STAGES][:, :], ACT.Copy, scale=W_SCALE).then_inc(s_whi, 1)

        def high(side, t):
            eng.wait_ge(s_tr[side], t.n + 1)
            wait(eng, s_hs if side == 0 else s_z, t.n * 2)
            eng.activation(hT[side][0][:, :].rearrange("p (h d) -> p h d", h=2), pT[:, :, 0:HALF], ACT.Copy,
                           scale=H_SCALE).then_inc(s_hi[side], 1)

        def normalise(kind, t, data):
            q = t.slot(2)
            eng.wait_ge(s_nm[kind], t.n + 1)
            eng.activation(data[:, :], data[:, :], ACT.Identity, bias=nm[:, kind, q:q + 1],
                           scale=rr[:, kind, q:q + 1]).then_inc(s_nrm[kind], 1)

        def body(i):
            if (t := i).inside(ET):
                wait(eng, s_agg, t.n - 3)
                for h in range(2):
                    eng.wait_ge(s_hs, t.n * 2 + (h + 1))
                    eng.activation(HS[t.slot(4)][:, h * HALF:(h + 1) * HALF], pZ[:, h, 0:HALF], ACT.Copy,
                                   scale=Z_SCALE).then_inc(s_hscopy, 1)
            if (t := i.of(1)).inside(ET):
                high(0, t)
            if (t := i.of(-1)).inside(ET):
                eng.wait_ge(s_dif, t.n + 1)
                wait(eng, s_wt, t.n - 1)
                eng.activation(ex[:, t.slot(2), :], dif[:, t.slot(2), :], ACT.Exp).then_inc(s_ex, 1)
            if (t := i.of(-2)).inside(ET):
                q = t.slot(2)
                eng.wait_ge(s_rs, t.n + 1)
                wait(eng, s_u, t.n - 1)
                if not t.fixed or t.r >= 1:
                    eng.wait_ge(s_carry[(t.r - 1) % 4], t.of(-1).turn(4) * 16 + 16)
                for h in range(H):
                    for a, z in ((h * HD, min((h + 1) * HD, VH)), (max(h * HD, VH), (h + 1) * HD)):
                        if a < z:
                            bank = a // VH
                            op = eng.activation(GA[q][:, a:z], pA[:, bank, a - bank * VH:z - bank * VH], ACT.Copy,
                                                scale=rs[:, q, h:h + 1])
                op.then_inc(s_ga, 1)
            if (t := i).inside(ET):
                wait(eng, s_logit, t.n - 1)
                for h in range(2):
                    eng.wait_ge(s_z, t.n * 2 + (h + 1))
                    eng.activation(ZC[t.slot(2)][:, h * HALF:(h + 1) * HALF], pZ[:, h, 0:HALF], ACT.Copy,
                                   scale=Z_SCALE).then_inc(s_zc, 1)
            if (t := i.of(1)).inside(ET):
                high(1, t)
            if (t := i.of(-2)).inside(ET):
                q = t.slot(2)
                eng.wait_ge(s_ga, t.n + 1)
                wait(eng, s_u0, t.n - 1)
                eng.activation(EX[q][:, :], GA[q][:, :], ACT.Exp).then_inc(s_e, 1)
            if (t := i.of(-3)).inside(ET):
                normalise(2, t, U[t.slot(4)])
            if (t := i.of(-4)).inside(ET) and final:
                normalise(3, t, U[t.slot(4)])

        pipeline(eng, body, -1, ET, LEAD, TAIL)

    @block.vector
    def _(eng):
        eng.wait_ge(s_vec, 16 * (7 if final else 5))
        for side in range(2):
            eng.tensor_scalar(bias_in[:, side, :], bias_in[:, side, :], 1.0 / Z_SCALE, None, ALU.mult).then_inc(
                s_brest, 1)
            eng.wait_ge(s_brest, 3 * side + 1)
            for part in range(3):
                eng.tensor_copy(bias_row[:, side, part, :], bias_in[:, side, :]).then_inc(s_bias, 1)
                if part < 2:
                    eng.wait_ge(s_bias, 3 * side + part + 1)
                    eng.tensor_tensor(bias_in[:, side, :], bias_in[:, side, :], bias_row[:, side, part, :],
                                      ALU.subtract).then_inc(s_brest, 1)
                    eng.wait_ge(s_brest, 3 * side + 2 + part)
        for n, (w, side, c) in enumerate(pieces):
            eng.wait_ge(s_whi, n + 1)
            eng.scalar_tensor_tensor(W[side][1][:, c, :], stage[n % STAGES][:, :], W_SCALE, W[side][0][:, c, :],
                                     ALU.mult, ALU.subtract).then_inc(s_wlo, 1)

        def moments(kind, t, data):
            q = t.slot(2)
            wait(eng, s_nrm[kind], t.n - 1)
            for h in range(2):
                op = eng.bn_stats(st[:, kind, q, h, :], data[:, h * HALF:(h + 1) * HALF])
            op.then_inc(s_bn[kind], 1)
            wait_apart(eng, s_passed, (s_bn[kind], t.n + 1))
            eng.bn_aggr(mv[:, kind, q, :], st[:, kind, q, :, :].rearrange("p a b -> p (a b)")).then_inc(s_mv[kind], 1)

        def normalise(kind, t, data):
            q = t.slot(2)
            eng.wait_ge(s_rb[kind], t.n + 1)
            eng.tensor_scalar(data[:, :], data[:, :], mv[:, kind, q, 0:1], rr[:, kind, q:q + 1], ALU.subtract,
                              ALU.mult).then_inc(s_nrm[kind], 1)

        def low(side, t):
            eng.wait_ge(s_hi[side], t.n + 1)
            eng.scalar_tensor_tensor(hT[side][1][:, :].rearrange("p (h d) -> p h d", h=2), pT[:, :, 0:HALF], H_SCALE,
                                     hT[side][0][:, :].rearrange("p (h d) -> p h d", h=2), ALU.mult,
                                     ALU.subtract).then_inc(s_lo[side], 1)

        def body(i):
            if (t := i.of(-1)).inside(ET):
                eng.wait_ge(s_zc, t.n * 2 + 2)
                z = ZC[t.slot(2)]
                eng.scalar_tensor_tensor(z[:, :], z[:, :], SLOPE, z[:, :], ALU.mult, ALU.max).then_inc(s_lrelu, 1)
            if (t := i.of(1)).inside(ET) and first:
                eng.wait_ge(s_xs[t.slot(2)], t.turn(2) * 16 + 16)
                moments(0, t, XS[t.slot(2)])
            if (t := i).inside(ET):
                low(1, t)
            if (t := i.of(-2)).inside(ET):
                c, q = t.slot(4), t.slot(2)
                eng.wait_ge(s_wt, t.n + 1)
                eng.wait_ge(s_hscopy, t.n * 2 + 2)
                eng.tensor_copy(HS[c][:, D:V], pS[:, 1, 0:H]).then_inc(s_wc, 1)
                eng.wait_ge(s_wc, t.n + 1)
                wait(eng, s_srow, t.n)
                if t.fixed and t.r == 0:
                    eng.wait_ge(s_const, 8)
                eng.tensor_tensor(HS[c][0:1, D:V], HS[c][0:1, D:V], srow[:, (t.r - 1) % 2, :], ALU.mult).then_inc(
                    s_w0, 1)
                eng.wait_ge(s_w0, t.n + 1)
                eng.wait_ge(s_carry[c], t.turn(4) * 16 + 16)
                eng.tensor_tensor(HS[c][:, 0:D].rearrange("p (h d) -> p h d", h=H),
                                  HS[c][:, 0:D].rearrange("p (h d) -> p h d", h=H),
                                  HS[c][:, D:V].unsqueeze(2).broadcast_to([P, H, HD]), ALU.mult).then_inc(s_wv, 1)
                wait(eng, s_agg, t.n - 1)
                eng.tensor_scalar(M[q][:, 1:P], key_row[:, bass.ds(t.n * EPT + 1, EPT)],
                                  key_col[:, bass.ds(t.n, 1)], None, ALU.is_equal).then_inc(s_m0, 1)
                eng.tensor_scalar(M[q][:, 0:1], key_row[:, bass.ds(t.n * EPT + EPT, 1)],
                                  key_col[:, bass.ds(t.n, 1)], None, ALU.is_equal).then_inc(s_m, 1)
            if (t := i.of(-1)).inside(ET):
                q = t.slot(2)
                eng.wait_ge(s_att, t.n + 1)
                wait(eng, s_lt, t.n - 1)
                eng.tensor_reduce(Lg[:, q, :], ZC[q][:, :].rearrange("p (h d) -> p h d", h=H), AX_X,
                                  ALU.add).then_inc(s_logit, 1)
            if (t := i.of(1)).inside(ET) and first:
                normalise(0, t, XS[t.slot(2)])
            if (t := i.of(-3)).inside(ET):
                c, q = t.slot(4), t.slot(2)
                eng.wait_ge(s_e, t.n + 1)
                wait(eng, s_put[c], t.turn(4) * 16)
                eng.scalar_tensor_tensor(U[c][:, :], EX[q][:, :], 1.0, XD[c][:, :], ALU.min, ALU.add).then_inc(s_u0, 1)
                eng.wait_ge(s_u0, t.n + 1)
                eng.scalar_tensor_tensor(U[c][:, :], GA[q][:, :], 0.0, U[c][:, :], ALU.max, ALU.add).then_inc(s_u, 1)
                eng.wait_ge(s_u, t.n + 1)
                moments(2, t, U[c])
            if (t := i.of(1)).inside(ET):
                low(0, t)
            if (t := i.of(-1)).inside(ET):
                q = t.slot(2)
                eng.wait_ge(s_lt, t.n + 1)
                eng.tensor_copy(LT[:, q, 1:P], pS[0:H, 0, 1:P]).then_inc(s_ltc, 1)
                if t.fixed and t.r == 0:
                    eng.wait_ge(s_const, 8)
                eng.wait_ge(s_ltc, t.n + 1)
                at = t.n * EPT
                eng.tensor_copy(ahead[:, q, :], border[:, bass.ds(at + 1, P)]).then_inc(s_ahead, 1)
                eng.tensor_tensor_scan(scan[:, q, 0, :], border[:, bass.ds(at, P)], LT[:, q, :], FAR, ALU.add,
                                       ALU.max).then_inc(s_fwd, 1)
                eng.wait_ge(s_fwd, t.n + 1)
                eng.wait_ge(s_ahead, t.n + 1)
                eng.tensor_tensor_scan(scan[:, q, 1, :][:, ::-1], ahead[:, q, ::-1],
                                       scan[:, q, 0, :][:, ::-1], FAR, ALU.add, ALU.max).then_inc(s_max, 1)
                eng.wait_ge(s_max, 2 * t.n + 1)
                wait(eng, s_ex, t.n - 1)
                eng.tensor_tensor(dif[:, q, :], LT[:, q, :], scan[:, q, 1, :], ALU.subtract).then_inc(s_dif, 1)
                eng.tensor_copy(LT[:, (t.r + 1) % 2, 0:1], scan[:, q, 1, P - 1:P]).then_inc(s_max, 1)
                eng.wait_ge(s_max, 2 * t.n + 2)
            if (t := i.of(-2)).inside(ET):
                q = t.slot(2)
                eng.wait_ge(s_agg, t.n + 1)
                off = D - VH
                eng.tensor_copy(srow[:, q, :], pA[0:1, 1, off:off + H]).then_inc(s_srow, 1)
                wait(eng, s_ga, t.n - 1)
                eng.reciprocal(rs[:, q, :], pA[:, 1, off:off + H]).then_inc(s_rs, 1)
            if (t := i.of(-4)).inside(ET):
                u = U[t.slot(4)]
                eng.wait_ge(s_yw, t.n + 1)
                eng.tensor_tensor(u[:, :], u[:, :], b_v[:, :], ALU.add).then_inc(s_y, 1)
                if final:
                    eng.wait_ge(s_y, t.n + 1)
                    moments(3, t, u)
            if (t := i.of(1)).inside(ET) and first:
                eng.wait_ge(s_xd[t.slot(4)], t.turn(4) * 16 + 16)
                moments(1, t, XD[t.slot(4)])
            if (t := i.of(-5)).inside(ET) and final:
                u, q = U[t.slot(4)], t.slot(2)
                eng.wait_ge(s_ow, t.n + 1)
                eng.tensor_tensor(u[:, :], u[:, :], ob_v[:, :], ALU.add).then_inc(s_ob, 1)
                eng.wait_ge(s_ob, t.n + 1)
                eng.wait_ge(s_xr[q], t.turn(2) * 16 + 16)
                eng.tensor_tensor(u[:, :], u[:, :], XR[q][:, :], ALU.add).then_inc(s_x1, 1)
            if (t := i.of(1)).inside(ET) and first:
                normalise(1, t, XD[t.slot(4)])

        pipeline(eng, body, -1, ET, LEAD, TAIL)


_INS = ['x', 'src', 'dst', 'L0_gnn_Wsrc', 'L0_gnn_bsrc', 'L0_gnn_Wdst', 'L0_gnn_bdst', 'L0_gnn_attn', 'L0_gnn_ln_w',
        'L0_gnn_ln_b', 'L0_gnn_on_w', 'L0_gnn_on_b', 'L0_ffn_w1', 'L0_ffn_b1', 'L0_ffn_alpha_w1', 'L0_ffn_alpha_a1',
        'L0_ffn_w2', 'L0_ffn_b2', 'L0_ffn_alpha_w2', 'L0_ffn_alpha_a2']
_OUTS = [((10000, 768), 'float32')]


def kernel(**inputs):
    import numpy as _np
    import concourse.bacc as _bacc
    from concourse import mybir as _mybir
    from concourse.bass_utils import run_bass_kernel_spmd as _run

    nc = _bacc.Bacc("TRN2", target_bir_lowering=False, num_devices=1)
    arrays, args = {}, []
    for name in _INS:
        a = _np.ascontiguousarray(inputs[name])
        arrays[f"in_{name}_dram"] = a
        args.append(nc.dram_tensor(f"in_{name}_dram", a.shape, _mybir.dt.from_np(a.dtype), kind="ExternalInput").ap())
    for i, (shape, dtype) in enumerate(_OUTS):
        dt = _mybir.dt.from_np(_np.dtype(dtype))
        args.append(nc.dram_tensor(f"out_{i}_dram", shape, dt, kind="ExternalOutput").ap())
    gat_and_quantised_ffn(nc, *args)
    r = _run(nc, [arrays], core_ids=[0])
    got = tuple(r.results[0][f"out_{i}_dram"] for i in range(len(_OUTS)))
    return got[0]
```
